# Optimizing a Trainium2 kernel written in Bass

```python
import numpy as np
import jax
import jax.numpy as jnp

def _softmax(x, axis=-1):
    return jax.nn.softmax(x, axis=axis)

def _gelu(x):
    return jax.nn.gelu(x, approximate=True)

def _silu(x):
    return jax.nn.silu(x)

def _sigmoid(x):
    return jax.nn.sigmoid(x)

def _layernorm(x, axis=-1, eps=1e-05):
    m = jnp.mean(x, axis=axis, keepdims=True)
    v = jnp.var(x, axis=axis, keepdims=True)
    return (x - m) / jnp.sqrt(v + eps)

def _scatter_add(tgt, idx, src, axis=0):
    return tgt.at[idx].add(src)

def _segment_sum(src, seg, n):
    return jax.ops.segment_sum(src, seg, n)
kernel_name = 'mk_gnn_resnorm_d1_gnn_r8_4a25e2'

def setup_inputs(seed: int=0):
    np.random.seed(seed)
    _w = jnp.asarray

    def _rec_inputs():
        import jax
        import jax.numpy as jnp
        _gk = jax.random.key(seed)
        x = -0.0005121 + 1.001 * jax.random.normal(jax.random.fold_in(_gk, 1), (12500, 64), jnp.float32)
        src = jax.random.randint(jax.random.fold_in(_gk, 2), (400000,), 0, 12500, jnp.int32)
        dst = jnp.minimum((12500 * jax.random.uniform(jax.random.fold_in(_gk, 3), (400000,)) ** 2.0).astype(jnp.int32), 99999)
        _o = jnp.argsort(dst, stable=True)
        src = src[_o]
        dst = dst[_o]
        edge_attr_64 = -8.16379e-05 + 0.999858 * jax.random.normal(jax.random.fold_in(_gk, 12), (400000, 64), jnp.float32)
        return (x, src, dst, edge_attr_64)
    x, src, dst, edge_attr_64 = _rec_inputs()

    def _L0_gnn_setup():
        import jax, jax.numpy as jnp
        import numpy as np
        N_NODES = 6250
        N_EDGES = 200000
        HID = 64
        key = jax.random.key(seed)
        ks = jax.random.split(key, 8)
        node_feat = jax.random.normal(ks[0], (N_NODES, HID), dtype=jnp.float32)
        edge_feat = jax.random.normal(ks[1], (N_EDGES, HID), dtype=jnp.float32)
        src = jax.random.randint(ks[2], (N_EDGES,), 0, N_NODES, dtype=jnp.int32)
        dst = jax.random.randint(ks[3], (N_EDGES,), 0, N_NODES, dtype=jnp.int32)
        s1 = 1.0 / np.sqrt(HID)
        s2 = 1.0 / np.sqrt(2 * HID)
        W1 = jax.random.uniform(ks[4], (HID, 2 * HID), jnp.float32, -s1, s1)
        b1 = jax.random.uniform(ks[5], (2 * HID,), jnp.float32, -s1, s1)
        W2 = jax.random.uniform(ks[6], (2 * HID, HID), jnp.float32, -s2, s2)
        b2 = jax.random.uniform(ks[7], (HID,), jnp.float32, -s2, s2)
        return {'node_feat': node_feat, 'edge_feat': edge_feat, 'src': src, 'dst': dst, 'W1': W1, 'b1': b1, 'W2': W2, 'b2': b2}
    _L0_gnn_all = _L0_gnn_setup()
    _L0_gnn_in = {k: v for k, v in _L0_gnn_all.items() if k in ('W1', 'b1', 'W2', 'b2')}
    del _L0_gnn_all
    return {'x': x, 'src': src, 'dst': dst, 'edge_attr_64': edge_attr_64, 'L0_gnn_W1': _L0_gnn_in['W1'], 'L0_gnn_b1': _L0_gnn_in['b1'], 'L0_gnn_W2': _L0_gnn_in['W2'], 'L0_gnn_b2': _L0_gnn_in['b2']}

def reference(x, src, dst, edge_attr_64, L0_gnn_W1, L0_gnn_b1, L0_gnn_W2, L0_gnn_b2):
    import jax
    import jax.numpy as jnp

    def _L0_gnn_ref(node_feat, edge_feat, src, dst, W1, b1, W2, b2):
        import jax, jax.numpy as jnp
        import numpy as np
        N_NODES = 6250
        N_EDGES = 200000
        HID = 64
        msg = node_feat[src] + edge_feat
        agg = jax.ops.segment_sum(msg, dst, num_segments=node_feat.shape[0])
        h = jax.nn.relu(agg @ W1 + b1)
        return h @ W2 + b2
    x = _layernorm(x + _L0_gnn_ref(x, edge_attr_64, src, dst, L0_gnn_W1, L0_gnn_b1, L0_gnn_W2, L0_gnn_b2), axis=-1)
    return x

_drawn_inputs = setup_inputs


def setup_inputs(seed=0):
    import zlib

    import numpy as np

    out = dict(_drawn_inputs(seed))
    spreads = {}
    factors = {'L0_gnn_b1': 3.143}
    for name, (base, spread) in spreads.items():
        noise = np.random.default_rng([zlib.crc32(name.encode()), seed]).standard_normal(out[name].shape)
        drawn = base * np.exp(spread * noise) if base else spread * noise
        out[name] = jnp.asarray(drawn.astype(out[name].dtype))
    for name, factor in factors.items():
        out[name] = (out[name] * factor).astype(out[name].dtype)
    return out
```

```python
import numpy as np
from contextlib import ExitStack

import concourse.bass as bass
from concourse import mybir

P = 128
HALF_EPS = 1e-5


def build(nc, x, src, dst, edge_attr, w1, b1, w2, b2, out):
    f32, i32, bf16 = mybir.dt.float32, mybir.dt.int32, mybir.dt.bfloat16
    ALU, ACT, AX = mybir.AluOpType, mybir.ActivationFunctionType, mybir.AxisListType

    N, D = x.shape
    E = src.shape[0]
    HID = w1.shape[1]
    TILES = 5
    SLOTS = 5
    CHUNK = P * TILES
    NCH = E // CHUNK
    TURNS = NCH // SLOTS
    assert TILES == SLOTS and NCH * CHUNK == E and TURNS * SLOTS == NCH and TURNS <= P
    SHIFT = 6
    WIN = 1 << SHIFT
    NWIN = -(-N // WIN)
    NPAD = N + WIN
    NODE_P, NODE_I = 125, 4
    BLOCK = NODE_P * NODE_I
    NBLK = N // BLOCK
    BTURNS = NBLK // SLOTS
    assert NBLK * BLOCK == N and BTURNS * SLOTS == NBLK

    edge_v = edge_attr.rearrange("(c p j) f -> c p (j f)", p=P, j=TILES)
    src_v = src.rearrange("(t e) -> t e", t=TURNS)
    dst_v = dst.rearrange("(t e) -> t e", t=TURNS)
    x_v = x.rearrange("(b p i) f -> p b (i f)", p=NODE_P, i=NODE_I)
    out_v = out.rearrange("(b p i) f -> b p (i f)", p=NODE_P, i=NODE_I)
    row_dram = nc.dram_tensor("chunk_rows", (2, NCH), i32, kind="Internal").ap()

    with ExitStack() as ctx:
        def sb(name, shape, dt=f32):
            return ctx.enter_context(nc.sbuf_tensor(name, shape, dt))

        def sem(name):
            return ctx.enter_context(nc.semaphore(name))

        ident = sb("ident", [P, P])
        iota_row = sb("iota_row", [P, WIN])
        win_start = sb("win_start", [P, NWIN])
        dst_i = sb("dst_i", [TURNS, SLOTS * CHUNK], i32)
        src_i = sb("src_i", [TURNS, SLOTS * CHUNK], i32)
        src_f = sb("src_f", [TURNS, SLOTS * CHUNK])
        rel = sb("rel", [TURNS, SLOTS * CHUNK])
        least = sb("least", [TURNS, SLOTS])
        most = sb("most", [TURNS, SLOTS])
        span = sb("span", [TURNS, SLOTS])
        least_i = sb("least_i", [TURNS, SLOTS], i32)
        span_i = sb("span_i", [TURNS, SLOTS], i32)
        nwin_i = sb("nwin_i", [TURNS, SLOTS], i32)
        base_row = sb("base_row", [1, NCH], i32)
        nwin_row = sb("nwin_row", [1, NCH], i32)
        scan = [sb("scan0", [1, NCH]), sb("scan1", [1, NCH])]
        first_row = sb("first_row", [1, NCH + 1], i32)
        final_row = sb("final_row", [1, NCH], i32)
        rel_t = sb("rel_t", [P, NCH * TILES])
        idx_t = sb("idx_t", [P, NCH * TILES], i32)
        idx = [sb(f"idx{s}", [P, TILES], i32) for s in range(SLOTS)]
        msg = [sb(f"msg{s}", [P, TILES * D]) for s in range(SLOTS)]
        onehot = [sb(f"onehot{s}", [P, TILES * WIN]) for s in range(SLOTS)]
        agg = sb("agg", [D, NPAD])
        x_sb = sb("x_sb", [NODE_P, NBLK * NODE_I * D])
        w1_sb = sb("w1_sb", [D, HID])
        w2_sb = sb("w2_sb", [HID, D])
        b1_sb = sb("b1_sb", [HID, 1])
        b2_sb = sb("b2_sb", [1, D])
        ones = sb("ones", [1, NODE_P])
        eps = sb("eps", [NODE_P, 1])
        hid = [sb(f"hid{s}", [HID, BLOCK]) for s in range(2)]
        res = [sb(f"res{s}", [NODE_P, NODE_I, D]) for s in range(2)]
        cen = [sb(f"cen{s}", [NODE_P, NODE_I, D]) for s in range(2)]
        sq = [sb(f"sq{s}", [NODE_P, NODE_I, D]) for s in range(2)]
        tot = [sb(f"tot{s}", [NODE_P, NODE_I]) for s in range(2)]
        var = [sb(f"var{s}", [NODE_P, NODE_I]) for s in range(2)]
        std = [sb(f"std{s}", [NODE_P, NODE_I]) for s in range(2)]
        rstd = [sb(f"rstd{s}", [NODE_P, NODE_I]) for s in range(2)]
        outb = [sb(f"outb{s}", [NODE_P, NODE_I, D]) for s in range(2)]

        bank = [ctx.enter_context(nc.psum_tensor(f"bank{i}", [P, 512], f32)) for i in range(8)]
        iota_ps = bank[7][:, 0:WIN]
        win_ps = [bank[s][0:D, 0:WIN] for s in range(SLOTS)]
        src_ps = [bank[k][:, :].rearrange("p (k t) -> p k t", t=P) for k in (0, 1)]
        dst_ps = [bank[k][:, :].rearrange("p (k t) -> p k t", t=P) for k in (2, 3)]
        hid_ps = [bank[0][:, 0:BLOCK], bank[1][:, 0:BLOCK]]
        y_ps = [bank[2][0:NODE_P, 0:NODE_I * D], bank[3][0:NODE_P, 0:NODE_I * D]]

        consts_made = sem("consts_made")
        iota_ready = sem("iota_ready")
        dst_in = sem("dst_in")
        src_in = sem("src_in")
        dst_rel = sem("dst_rel")
        prep = sem("prep")
        rows_out = sem("rows_out")
        rows_in = sem("rows_in")
        rows_ready = sem("rows_ready")
        src_cast = sem("src_cast")
        src_turned = sem("src_turned")
        src_taken = sem("src_taken")
        dst_turned = sem("dst_turned")
        dst_taken = sem("dst_taken")
        scanned = sem("scanned")
        idx_ready = [sem(f"idx_ready{s}") for s in range(SLOTS)]
        edges_in = [sem(f"edges_in{s}") for s in range(SLOTS)]
        gathered = [sem(f"gathered{s}") for s in range(SLOTS)]
        onehot_ready = sem("onehot_ready")
        summed = sem("summed")
        added = sem("added")
        weights_in = sem("weights_in")
        x_in = sem("x_in")
        hid_summed = sem("hid_summed")
        hid_ready = sem("hid_ready")
        y_summed = sem("y_summed")
        res_ready = sem("res_ready")
        tot_ready = sem("tot_ready")
        cen_ready = sem("cen_ready")
        sq_ready = sem("sq_ready")
        rstd_ready = sem("rstd_ready")
        var_ready = sem("var_ready")
        std_ready = sem("std_ready")
        out_ready = sem("out_ready")
        stored = [sem("stored0"), sem("stored1")]

        block = ctx.enter_context(nc.Block())
        NTR = SLOTS * TILES
        GROUPS = [(k, min(4, NTR - k)) for k in range(0, NTR, 4)]

        @block.sync
        def _(sp):
            sp.dma_start(dst_i[:, :], dst_v).then_inc(dst_in, 16)
            sp.dma_start(src_i[:, :], src_v).then_inc(src_in, 16)
            sp.dma_start(w1_sb[:, :], w1).then_inc(weights_in, 16)
            sp.dma_start(w2_sb[:, :], w2).then_inc(weights_in, 16)
            sp.dma_start(b1_sb[:, :], b1.rearrange("(h o) -> h o", o=1)).then_inc(weights_in, 16)
            sp.dma_start(b2_sb[:, :], b2.rearrange("(o f) -> o f", o=1)).then_inc(weights_in, 16)
            sp.wait_ge(prep, 5)
            sp.dma_start(row_dram[0].rearrange("(t s) -> t s", s=SLOTS), least_i[:, :]).then_inc(rows_out, 16)
            sp.dma_start(row_dram[1].rearrange("(t s) -> t s", s=SLOTS), nwin_i[:, :]).then_inc(rows_out, 16)
            sp.wait_ge(rows_out, 32)
            sp.dma_start(base_row[:, :], row_dram[0:1, :]).then_inc(rows_in, 16)
            sp.dma_start(nwin_row[:, :], row_dram[1:2, :]).then_inc(rows_in, 16)
            for s in range(SLOTS):
                sp.dma_start(msg[s][:, :], edge_v[s]).then_inc(edges_in[s], 16)
            sp.dma_start(x_sb[:, :].rearrange("p (b k) -> p b k", b=NBLK), x_v).then_inc(x_in, 16)
            sp.wait_ge(rows_ready, 2)
            with sp.Fori(1, TURNS) as t:
                for s in range(SLOTS):
                    before = sp.value_load(first_row[0:1, bass.ds(t * SLOTS + (s - SLOTS + 1), 1)],
                                           min_val=0, max_val=NCH * NWIN)
                    sp.wait_ge(summed, before)
                    sp.dma_start(msg[s][:, :], edge_v[t * SLOTS + s]).then_inc(edges_in[s], 16)
            with sp.Fori(0, NBLK - 1, 2) as b:
                for k in range(2):
                    sp.wait_ge(out_ready, b + (k + 1))
                    sp.dma_start(out_v[b + k], outb[k][:, :, :].rearrange("p i f -> p (i f)")).then_inc(stored[k], 16)
            sp.wait_ge(out_ready, NBLK)
            sp.dma_start(out_v[NBLK - 1], outb[0][:, :, :].rearrange("p i f -> p (i f)")).then_inc(stored[0], 16)
            sp.wait_ge(stored[0], 16 * (NBLK // 2 + 1))
            sp.wait_ge(stored[1], 16 * (NBLK // 2))

        @block.gpsimd
        def _(pool):
            nc.gpsimd.memset(ident[:, :], 0.0).then_inc(consts_made, 1)
            nc.gpsimd.iota(iota_row[:, :], pattern=[[1, WIN]], base=0, channel_multiplier=0,
                           allow_small_or_imprecise_dtypes=True).then_inc(consts_made, 1)
            nc.gpsimd.iota(win_start[:, :], pattern=[[WIN, NWIN]], base=0, channel_multiplier=0,
                           allow_small_or_imprecise_dtypes=True).then_inc(consts_made, 1)
            nc.gpsimd.memset(ones[:, :], 1.0).then_inc(consts_made, 1)
            nc.gpsimd.memset(eps[:, :], HALF_EPS).then_inc(consts_made, 1)
            nc.gpsimd.memset(agg[:, :], 0.0).then_inc(added, 1)
            pool.wait_ge(consts_made, 5)
            nc.gpsimd.affine_select(out=ident[:, :], in_=ident[:, :], compare_op=ALU.not_equal, fill=1.0, base=0,
                                    pattern=[[-1, P]], channel_multiplier=1).then_inc(consts_made, 1)
            with pool.Fori(16, 16 * TURNS + 1, 16) as due:
                for s in range(SLOTS):
                    pool.wait_ge(consts_made, 6)
                    pool.wait_ge(edges_in[s], due)
                    pool.wait_ge(idx_ready[s], due)
                    for j in range(TILES):
                        pool.indirect_dma_start(msg[s][:, j * D:(j + 1) * D], None, x,
                                                bass.IndirectOffsetOnAxis(ap=idx[s][:, j:j + 1], axis=0),
                                                compute_op=ALU.add).then_inc(gathered[s], 16)

        def tiles_of(flat):
            return flat[:, :].rearrange("t (s p j) -> t s j p", s=SLOTS, j=TILES)

        @block.scalar
        def _(act):
            act.wait_ge(src_in, 16)
            nc.scalar.copy(src_f[:, :], src_i[:, :]).then_inc(src_cast, 1)
            act.wait_ge(consts_made, 6)
            nc.scalar.copy(iota_ps, iota_row[:, :]).then_inc(iota_ready, 1)
            for g, (k, n) in enumerate(GROUPS):
                act.wait_ge(src_turned, g + 1)
                nc.scalar.copy(idx_t[:, :].rearrange("p (t k) -> p k t", k=NTR)[:, k:k + n, :],
                               src_ps[g % 2][:, 0:n, 0:TURNS]).then_inc(src_taken, 1)
            act.wait_ge(src_taken, len(GROUPS))
            for s in range(SLOTS):
                nc.scalar.copy(idx[s][:, :], idx_t[:, s * TILES:(s + 1) * TILES]).then_inc(idx_ready[s], 16)
            with act.Fori(1, TURNS) as t:
                for s in range(SLOTS):
                    act.wait_ge(gathered[s], t * (16 * TILES))
                    nc.scalar.copy(idx[s][:, :],
                                   idx_t[:, bass.ds((t * SLOTS + s) * TILES, TILES)]).then_inc(idx_ready[s], 16)
            act.wait_ge(weights_in, 64)

            def relu(b, k, first=False):
                act.wait_ge(hid_summed, b + 1)
                if not first:
                    act.wait_ge(y_summed, b - 1)
                nc.scalar.activation(hid[k][:, :], hid_ps[k], ACT.Relu, bias=b1_sb[:, 0:1]).then_inc(hid_ready, 1)

            def root(b, k):
                act.wait_ge(var_ready, b + 1)
                nc.scalar.activation(std[k][:, :], var[k][:, :], ACT.Sqrt, bias=eps[:, 0:1],
                                     scale=1.0 / D).then_inc(std_ready, 1)

            relu(0, 0, True)
            relu(1, 1, True)
            with act.Fori(0, NBLK - 3, 2) as b:
                for k in range(2):
                    root(b + k, k)
                    relu(b + (k + 2), k)
            root(NBLK - 3, 0)
            relu(NBLK - 1, 0)
            root(NBLK - 2, 1)
            root(NBLK - 1, 0)

        @block.vector
        def _(dve):
            dve.wait_ge(dst_in, 16)
            chunks = dst_i[:, :].rearrange("t (s e) -> t s e", s=SLOTS)
            nc.vector.tensor_reduce(least[:, :], chunks, axis=AX.X, op=ALU.min).then_inc(prep, 1)
            nc.vector.tensor_reduce(most[:, :], chunks, axis=AX.X, op=ALU.max).then_inc(prep, 1)
            dve.wait_ge(prep, 2)
            nc.vector.tensor_copy(least_i[:, :], least[:, :]).then_inc(prep, 1)
            nc.vector.tensor_tensor(span_i[:, :], most[:, :], least[:, :], ALU.subtract).then_inc(prep, 1)
            dve.wait_ge(prep, 4)
            nc.vector.tensor_scalar(nwin_i[:, :], span_i[:, :], SHIFT, None, ALU.arith_shift_right).then_inc(prep, 1)
            nc.vector.tensor_tensor(rel[:, :].rearrange("t (s e) -> t s e", s=SLOTS), chunks,
                                    least[:, :].unsqueeze(2).broadcast_to([TURNS, SLOTS, CHUNK]),
                                    ALU.subtract).then_inc(dst_rel, 1)
            for g, (k, n) in enumerate(GROUPS):
                dve.wait_ge(dst_turned, g + 1)
                nc.vector.tensor_copy(rel_t[:, :].rearrange("p (t k) -> p k t", k=NTR)[:, k:k + n, :],
                                      dst_ps[g % 2][:, 0:n, 0:TURNS]).then_inc(dst_taken, 1)
            dve.wait_ge(rows_in, 32)
            nc.vector.tensor_scalar(scan[0][:, :], nwin_row[:, :], 1.0, None, ALU.add).then_inc(scanned, 1)
            steps, at = 1, 1
            while at < NCH:
                dve.wait_ge(scanned, steps)
                a, b = scan[(steps - 1) % 2], scan[steps % 2]
                nc.vector.tensor_copy(b[:, 0:at], a[:, 0:at])
                nc.vector.tensor_tensor(b[:, at:], a[:, at:], a[:, 0:NCH - at], ALU.add).then_inc(scanned, 1)
                steps, at = steps + 1, 2 * at
            dve.wait_ge(scanned, steps)
            nc.vector.memset(first_row[:, 0:1], 0)
            nc.vector.tensor_copy(first_row[:, 1:], scan[(steps - 1) % 2][:, :]).then_inc(rows_ready, 1)
            nc.vector.tensor_scalar(final_row[:, :], scan[(steps - 1) % 2][:, :], -1.0, None,
                                    ALU.add).then_inc(rows_ready, 1)
            dve.wait_ge(rows_ready, 2)
            dve.wait_ge(dst_taken, len(GROUPS))
            dve.wait_ge(iota_ready, 1)
            dve.wait_ge(consts_made, 6)

            def mark(c, s, w):
                return nc.vector.scalar_tensor_tensor(
                    out=onehot[s][:, :].rearrange("p (j n) -> p j n", j=TILES),
                    in0=iota_ps.unsqueeze(1).broadcast_to([P, TILES, WIN]), scalar=win_start[:, bass.ds(w, 1)],
                    in1=rel_t[:, bass.ds(c * TILES, TILES)].unsqueeze(2).broadcast_to([P, TILES, WIN]),
                    op0=ALU.add, op1=ALU.is_equal).then_inc(onehot_ready, 1)

            def add(s, base, w, v):
                dve.wait_ge(summed, v + 1)
                dve.wait_ge(added, v + 1)
                at = agg[:, bass.ds((base + w * WIN).with_bounds(min_val=0, max_val=N - 1), WIN)]
                return nc.vector.tensor_tensor(at, at, win_ps[s], ALU.add).then_inc(added, 1)

            def chunk(t, s, pending):
                c = t * SLOTS + s
                first = dve.value_load(first_row[0:1, bass.ds(c, 1)], min_val=0, max_val=NCH * NWIN)
                final = dve.value_load(final_row[0:1, bass.ds(c, 1)], min_val=0, max_val=NCH * NWIN)
                base = dve.value_load(base_row[0:1, bass.ds(c, 1)], min_val=0, max_val=N - 1)
                mark(c, s, 0)
                if pending is not None:
                    add(*pending)
                with dve.If(first < final):
                    with dve.Fori(first, final) as v:
                        w = (v - first).with_bounds(min_val=0, max_val=NWIN - 2)
                        add(s, base, w, v)
                        mark(c, s, w + 1)
                return s, base, (final - first).with_bounds(min_val=0, max_val=NWIN - 1), final

            with dve.Fori(0, TURNS) as t:
                pending = None
                for s in range(SLOTS):
                    pending = chunk(t, s, pending)
                add(*pending)

            dve.wait_ge(x_in, 16)

            def residual(b, k):
                dve.wait_ge(y_summed, b + 1)
                xb = x_sb[:, bass.ds(b * (NODE_I * D), NODE_I * D)].rearrange("p (i f) -> p i f", i=NODE_I)
                nc.vector.tensor_tensor(res[k][:, :, :], y_ps[k].rearrange("p (i f) -> p i f", i=NODE_I), xb,
                                        ALU.add).then_inc(res_ready, 1)
                dve.wait_ge(res_ready, b + 1)
                nc.vector.tensor_reduce(tot[k][:, :], res[k][:, :, :], axis=AX.X, op=ALU.add).then_inc(tot_ready, 1)
                dve.wait_ge(tot_ready, b + 1)
                nc.vector.scalar_tensor_tensor(
                    out=cen[k][:, :, :], in0=tot[k][:, :].unsqueeze(2).broadcast_to([NODE_P, NODE_I, D]),
                    scalar=-1.0 / D, in1=res[k][:, :, :], op0=ALU.mult, op1=ALU.add).then_inc(cen_ready, 1)
                dve.wait_ge(cen_ready, b + 1)
                nc.vector.tensor_tensor(sq[k][:, :, :], cen[k][:, :, :], cen[k][:, :, :],
                                        ALU.mult).then_inc(sq_ready, 1)
                dve.wait_ge(sq_ready, b + 1)
                nc.vector.tensor_reduce(var[k][:, :], sq[k][:, :, :], axis=AX.X, op=ALU.add).then_inc(var_ready, 1)

            def scale(b, k, first=False):
                dve.wait_ge(std_ready, b + 1)
                nc.vector.reciprocal(rstd[k][:, :], std[k][:, :]).then_inc(rstd_ready, 1)
                dve.wait_ge(rstd_ready, b + 1)
                if not first:
                    dve.wait_ge(stored[k], (b - k) * 8)
                nc.vector.tensor_tensor(outb[k][:, :, :], cen[k][:, :, :],
                                        rstd[k][:, :].unsqueeze(2).broadcast_to([NODE_P, NODE_I, D]),
                                        ALU.mult).then_inc(out_ready, 1)

            residual(0, 0)
            residual(1, 1)
            scale(0, 0, True)
            residual(2, 0)
            scale(1, 1, True)
            residual(3, 1)
            with dve.Fori(2, NBLK - 3, 2) as b:
                for k in range(2):
                    scale(b + k, k)
                    residual(b + (k + 2), k)
            scale(NBLK - 3, 0)
            residual(NBLK - 1, 0)
            scale(NBLK - 2, 1)
            scale(NBLK - 1, 0)

        @block.tensor
        def _(pe):
            def turn(g, ps, flat, turned, taken):
                k, n = GROUPS[g]
                if g >= 2:
                    pe.wait_ge(taken, g - 1)
                for i in range(n):
                    s, j = divmod(k + i, TILES)
                    tr = nc.tensor.transpose(ps[g % 2][:, i, 0:TURNS], tiles_of(flat)[:, s, j, :],
                                             ident[0:TURNS, 0:TURNS])
                tr.then_inc(turned, 1)

            pe.wait_ge(src_cast, 1)
            pe.wait_ge(consts_made, 6)
            for g in range(len(GROUPS)):
                turn(g, src_ps, src_f, src_turned, src_taken)
                pe.wait_ge(dst_rel, 1)
                turn(g, dst_ps, rel, dst_turned, dst_taken)
            pe.wait_ge(src_taken, len(GROUPS))
            pe.wait_ge(dst_taken, len(GROUPS))
            pe.wait_ge(rows_ready, 2)
            with pe.Fori(16 * TILES, 16 * TILES * TURNS + 1, 16 * TILES) as due:
                for s in range(SLOTS):
                    c = (due // 16) + (s - TILES)
                    first = pe.value_load(first_row[0:1, bass.ds(c, 1)], min_val=0, max_val=NCH * NWIN)
                    after = pe.value_load(first_row[0:1, bass.ds(c + 1, 1)], min_val=1, max_val=NCH * NWIN)
                    pe.wait_ge(rows_ready, 2)
                    pe.wait_ge(gathered[s], due)
                    with pe.Fori(first, after) as v:
                        pe.wait_ge(onehot_ready, v + 1)
                        for j in range(TILES):
                            mm = nc.tensor.matmul(win_ps[s], msg[s][:, j * D:(j + 1) * D],
                                                  onehot[s][:, j * WIN:(j + 1) * WIN],
                                                  start=(j == 0), stop=(j == TILES - 1))
                        mm.then_inc(summed, 1)
            pe.wait_ge(weights_in, 64)
            total = pe.value_load(first_row[0:1, NCH:NCH + 1], min_val=0, max_val=NCH * NWIN)
            pe.wait_ge(added, total + 1)

            def hidden(b, k, first=False):
                if not first:
                    pe.wait_ge(hid_ready, b - 1)
                nc.tensor.matmul(hid_ps[k], w1_sb[:, :], agg[:, bass.ds(b * BLOCK, BLOCK)],
                                 start=True, stop=True).then_inc(hid_summed, 1)

            def project(b, k, first=False):
                pe.wait_ge(hid_ready, b + 1)
                if not first:
                    pe.wait_ge(res_ready, b - 1)
                for i in range(NODE_I):
                    y = y_ps[k][:, i * D:(i + 1) * D]
                    nc.tensor.matmul(y, hid[k][:, i::NODE_I], w2_sb[:, :], start=True, stop=False)
                    mm = nc.tensor.matmul(y, ones[:, :], b2_sb[:, :], start=False, stop=True)
                mm.then_inc(y_summed, 1)

            hidden(0, 0, True)
            hidden(1, 1, True)
            project(0, 0, True)
            hidden(2, 0)
            project(1, 1, True)
            hidden(3, 1)
            with pe.Fori(2, NBLK - 3, 2) as b:
                for k in range(2):
                    project(b + k, k)
                    hidden(b + (k + 2), k)
            project(NBLK - 3, 0)
            hidden(NBLK - 1, 0)
            project(NBLK - 2, 1)
            project(NBLK - 1, 0)


INPUTS = ["x", "src", "dst", "edge_attr_64", "L0_gnn_W1", "L0_gnn_b1", "L0_gnn_W2", "L0_gnn_b2"]


def kernel(**inputs):
    import concourse.bacc as bacc
    from concourse.bass_utils import run_bass_kernel_spmd

    nc = bacc.Bacc("TRN2", target_bir_lowering=False, num_devices=1)
    arrays, args = {}, []
    for name in INPUTS:
        a = np.ascontiguousarray(inputs[name])
        arrays[f"in_{name}"] = a
        args.append(nc.dram_tensor(f"in_{name}", a.shape, mybir.dt.from_np(a.dtype), kind="ExternalInput").ap())
    shape = inputs["x"].shape
    args.append(nc.dram_tensor("out_nodes", shape, mybir.dt.float32, kind="ExternalOutput").ap())
    build(nc, *args)
    r = run_bass_kernel_spmd(nc, [arrays], core_ids=[0])
    return r.results[0]["out_nodes"]
```
